# Optimizing a Trainium2 kernel written in Bass

```python
import numpy as np
import jax
import jax.numpy as jnp

def _softmax(x, axis=-1):
    return jax.nn.softmax(x, axis=axis)

def _gelu(x):
    return jax.nn.gelu(x, approximate=True)

def _silu(x):
    return jax.nn.silu(x)

def _sigmoid(x):
    return jax.nn.sigmoid(x)

def _layernorm(x, axis=-1, eps=1e-05):
    m = jnp.mean(x, axis=axis, keepdims=True)
    v = jnp.var(x, axis=axis, keepdims=True)
    return (x - m) / jnp.sqrt(v + eps)

def _scatter_add(tgt, idx, src, axis=0):
    return tgt.at[idx].add(src)

def _segment_sum(src, seg, n):
    return jax.ops.segment_sum(src, seg, n)
kernel_name = 'mk_dlrm_tower_d1_rec_r8_37f15b'

def setup_inputs(seed: int=0):
    np.random.seed(seed)
    _w = jnp.asarray

    def _rec_inputs():
        import jax
        import jax.numpy as jnp
        _tk = jax.random.key(seed)
        ids = jnp.stack([jax.random.randint(jax.random.fold_in(_tk, 200 + f), (512,), 0, v, jnp.int32) for f, v in enumerate([1000, 1250, 1250, 125000, 12500, 1000, 1000, 1000, 1250, 12500, 1250, 12500, 12500, 12500, 1000, 1000, 1250, 12500, 12500, 1250, 12500, 1250, 1250, 1250, 1000, 1000])], axis=1)
        tbl_0 = 0.05 * jax.random.normal(jax.random.fold_in(_tk, 500 + 0), (1000, 128), jnp.float32)
        tbl_1 = 0.05 * jax.random.normal(jax.random.fold_in(_tk, 500 + 1), (1250, 128), jnp.float32)
        tbl_2 = 0.05 * jax.random.normal(jax.random.fold_in(_tk, 500 + 2), (1250, 128), jnp.float32)
        tbl_3 = 0.05 * jax.random.normal(jax.random.fold_in(_tk, 500 + 3), (125000, 128), jnp.float32)
        tbl_4 = 0.05 * jax.random.normal(jax.random.fold_in(_tk, 500 + 4), (12500, 128), jnp.float32)
        tbl_5 = 0.05 * jax.random.normal(jax.random.fold_in(_tk, 500 + 5), (1000, 128), jnp.float32)
        tbl_6 = 0.05 * jax.random.normal(jax.random.fold_in(_tk, 500 + 6), (1000, 128), jnp.float32)
        tbl_7 = 0.05 * jax.random.normal(jax.random.fold_in(_tk, 500 + 7), (1000, 128), jnp.float32)
        tbl_8 = 0.05 * jax.random.normal(jax.random.fold_in(_tk, 500 + 8), (1250, 128), jnp.float32)
        tbl_9 = 0.05 * jax.random.normal(jax.random.fold_in(_tk, 500 + 9), (12500, 128), jnp.float32)
        tbl_10 = 0.05 * jax.random.normal(jax.random.fold_in(_tk, 500 + 10), (1250, 128), jnp.float32)
        tbl_11 = 0.05 * jax.random.normal(jax.random.fold_in(_tk, 500 + 11), (12500, 128), jnp.float32)
        tbl_12 = 0.05 * jax.random.normal(jax.random.fold_in(_tk, 500 + 12), (12500, 128), jnp.float32)
        tbl_13 = 0.05 * jax.random.normal(jax.random.fold_in(_tk, 500 + 13), (12500, 128), jnp.float32)
        tbl_14 = 0.05 * jax.random.normal(jax.random.fold_in(_tk, 500 + 14), (1000, 128), jnp.float32)
        tbl_15 = 0.05 * jax.random.normal(jax.random.fold_in(_tk, 500 + 15), (1000, 128), jnp.float32)
        tbl_16 = 0.05 * jax.random.normal(jax.random.fold_in(_tk, 500 + 16), (1250, 128), jnp.float32)
        tbl_17 = 0.05 * jax.random.normal(jax.random.fold_in(_tk, 500 + 17), (12500, 128), jnp.float32)
        tbl_18 = 0.05 * jax.random.normal(jax.random.fold_in(_tk, 500 + 18), (12500, 128), jnp.float32)
        tbl_19 = 0.05 * jax.random.normal(jax.random.fold_in(_tk, 500 + 19), (1250, 128), jnp.float32)
        tbl_20 = 0.05 * jax.random.normal(jax.random.fold_in(_tk, 500 + 20), (12500, 128), jnp.float32)
        tbl_21 = 0.05 * jax.random.normal(jax.random.fold_in(_tk, 500 + 21), (1250, 128), jnp.float32)
        tbl_22 = 0.05 * jax.random.normal(jax.random.fold_in(_tk, 500 + 22), (1250, 128), jnp.float32)
        tbl_23 = 0.05 * jax.random.normal(jax.random.fold_in(_tk, 500 + 23), (1250, 128), jnp.float32)
        tbl_24 = 0.05 * jax.random.normal(jax.random.fold_in(_tk, 500 + 24), (1000, 128), jnp.float32)
        tbl_25 = 0.05 * jax.random.normal(jax.random.fold_in(_tk, 500 + 25), (1000, 128), jnp.float32)
        _rk = jax.random.fold_in(_tk, 7)
        r_dense_features = -0.000520686 + 1.00062 * jax.random.normal(jax.random.fold_in(_rk, 101), (512, 128), jnp.float32)
        W_top1 = 0.0405887 * jax.random.normal(jax.random.fold_in(_tk, 801), (607, 512), jnp.float32)
        W_top2 = 0.0441942 * jax.random.normal(jax.random.fold_in(_tk, 802), (512, 256), jnp.float32)
        W_top3 = 0.0625 * jax.random.normal(jax.random.fold_in(_tk, 803), (256, 1), jnp.float32)
        b_top1 = jnp.zeros((512,), jnp.float32)
        b_top2 = jnp.zeros((256,), jnp.float32)
        return (r_dense_features, ids, tbl_0, tbl_1, tbl_2, tbl_3, tbl_4, tbl_5, tbl_6, tbl_7, tbl_8, tbl_9, tbl_10, tbl_11, tbl_12, tbl_13, tbl_14, tbl_15, tbl_16, tbl_17, tbl_18, tbl_19, tbl_20, tbl_21, tbl_22, tbl_23, tbl_24, tbl_25, W_top1, b_top1, W_top2, b_top2, W_top3)
    r_dense_features, ids, tbl_0, tbl_1, tbl_2, tbl_3, tbl_4, tbl_5, tbl_6, tbl_7, tbl_8, tbl_9, tbl_10, tbl_11, tbl_12, tbl_13, tbl_14, tbl_15, tbl_16, tbl_17, tbl_18, tbl_19, tbl_20, tbl_21, tbl_22, tbl_23, tbl_24, tbl_25, W_top1, b_top1, W_top2, b_top2, W_top3 = _rec_inputs()

    def _L0_rec_setup():
        import jax, jax.numpy as jnp
        import numpy as np
        F = 26
        N = F + 1
        _TRIU_I, _TRIU_J = np.triu_indices(N, k=1)
        key = jax.random.key(seed)
        k1, k2 = jax.random.split(key)
        B, D = (2048, 128)
        dense_features = jax.random.normal(k1, (B, D), dtype=jnp.float32)
        sparse_features = jax.random.normal(k2, (B, F, D), dtype=jnp.float32)
        return {'dense_features': dense_features, 'sparse_features': sparse_features}
    _L0_rec_all = _L0_rec_setup()
    _L0_rec_in = {k: v for k, v in _L0_rec_all.items() if k in ()}
    del _L0_rec_all
    return {'r_dense_features': r_dense_features, 'ids': ids, 'tbl_0': tbl_0, 'tbl_1': tbl_1, 'tbl_2': tbl_2, 'tbl_3': tbl_3, 'tbl_4': tbl_4, 'tbl_5': tbl_5, 'tbl_6': tbl_6, 'tbl_7': tbl_7, 'tbl_8': tbl_8, 'tbl_9': tbl_9, 'tbl_10': tbl_10, 'tbl_11': tbl_11, 'tbl_12': tbl_12, 'tbl_13': tbl_13, 'tbl_14': tbl_14, 'tbl_15': tbl_15, 'tbl_16': tbl_16, 'tbl_17': tbl_17, 'tbl_18': tbl_18, 'tbl_19': tbl_19, 'tbl_20': tbl_20, 'tbl_21': tbl_21, 'tbl_22': tbl_22, 'tbl_23': tbl_23, 'tbl_24': tbl_24, 'tbl_25': tbl_25, 'W_top1': W_top1, 'b_top1': b_top1, 'W_top2': W_top2, 'b_top2': b_top2, 'W_top3': W_top3}

def reference(r_dense_features, ids, tbl_0, tbl_1, tbl_2, tbl_3, tbl_4, tbl_5, tbl_6, tbl_7, tbl_8, tbl_9, tbl_10, tbl_11, tbl_12, tbl_13, tbl_14, tbl_15, tbl_16, tbl_17, tbl_18, tbl_19, tbl_20, tbl_21, tbl_22, tbl_23, tbl_24, tbl_25, W_top1, b_top1, W_top2, b_top2, W_top3):
    import jax
    import jax.numpy as jnp

    def _L0_rec_ref(dense_features, sparse_features):
        import jax, jax.numpy as jnp
        import numpy as np
        F = 26
        N = F + 1
        _TRIU_I, _TRIU_J = np.triu_indices(N, k=1)
        combined = jnp.concatenate([dense_features[:, None, :], sparse_features], axis=1)
        interactions = jnp.einsum('bnd,bmd->bnm', combined, combined)
        interactions_flat = interactions[:, _TRIU_I, _TRIU_J]
        return jnp.concatenate([dense_features, interactions_flat], axis=1)
    e = jnp.stack([tbl_0[ids[:, 0]], tbl_1[ids[:, 1]], tbl_2[ids[:, 2]], tbl_3[ids[:, 3]], tbl_4[ids[:, 4]], tbl_5[ids[:, 5]], tbl_6[ids[:, 6]], tbl_7[ids[:, 7]], tbl_8[ids[:, 8]], tbl_9[ids[:, 9]], tbl_10[ids[:, 10]], tbl_11[ids[:, 11]], tbl_12[ids[:, 12]], tbl_13[ids[:, 13]], tbl_14[ids[:, 14]], tbl_15[ids[:, 15]], tbl_16[ids[:, 16]], tbl_17[ids[:, 17]], tbl_18[ids[:, 18]], tbl_19[ids[:, 19]], tbl_20[ids[:, 20]], tbl_21[ids[:, 21]], tbl_22[ids[:, 22]], tbl_23[ids[:, 23]], tbl_24[ids[:, 24]], tbl_25[ids[:, 25]]], axis=1)
    z = _L0_rec_ref(r_dense_features, e)
    z = z.reshape(z.shape[0], -1)
    h = jnp.concatenate([z, r_dense_features], axis=1)
    h = jnp.maximum(h @ W_top1 + b_top1, 0.0)
    h = jnp.maximum(h @ W_top2 + b_top2, 0.0)
    y = h @ W_top3
    return y

_drawn_inputs = setup_inputs


def setup_inputs(seed=0):
    import zlib

    import numpy as np

    out = dict(_drawn_inputs(seed))
    spreads = {'b_top1': (0.0, 0.1), 'b_top2': (0.0, 0.1)}
    factors = {}
    for name, (base, spread) in spreads.items():
        noise = np.random.default_rng([zlib.crc32(name.encode()), seed]).standard_normal(out[name].shape)
        drawn = base * np.exp(spread * noise) if base else spread * noise
        out[name] = jnp.asarray(drawn.astype(out[name].dtype))
    for name, factor in factors.items():
        out[name] = (out[name] * factor).astype(out[name].dtype)
    return out
```

```python
from contextlib import ExitStack

import concourse.bass as bass
from concourse import mybir

F32 = mybir.dt.float32
F32R = mybir.dt.float32r
I32 = mybir.dt.int32
ALU = mybir.AluOpType
ACT = mybir.ActivationFunctionType

BATCH = 512
D = 128
VOCAB = [1000, 1250, 1250, 125000, 12500, 1000, 1000, 1000, 1250, 12500, 1250, 12500, 12500,
         12500, 1000, 1000, 1250, 12500, 12500, 1250, 12500, 1250, 1250, 1250, 1000, 1000]
N_FIELDS = len(VOCAB)
N = N_FIELDS + 1
NJ = N - 1
ONEHOT_ROWS = 1000
ONEHOT = [f for f in range(N_FIELDS) if VOCAB[f] == ONEHOT_ROWS][:8]
K = len(ONEHOT)
GATHERED = [f for f in range(N_FIELDS) if f not in ONEHOT]
VC = 8
VP = ONEHOT_ROWS // VC

TILE = 128
TILES = BATCH // TILE
PER_BANK = 4
GROUPS = [GATHERED[g:g + PER_BANK] for g in range(0, len(GATHERED), PER_BANK)]
GB = 16
UNIT = 2 * GB
UNITS = TILE // UNIT
CHUNKS = -(-NJ // 4)
H1, H2 = 512, 256
M1, M2 = H1 // 128, H2 // 128
LAST = 32 * (NJ - 4 * (CHUNKS - 1))


def tower(nc, dense_t, ids, onehot_ids, row_of, tables, w_dense_a, w_dense_b, w_pairs, b1, w2, b2, w3,
          ident_in, out):
    with ExitStack() as ctx:
        def sb(name, shape, dt=F32):
            return ctx.enter_context(nc.sbuf_tensor(name, shape, dt))

        def psum(name, shape):
            return ctx.enter_context(nc.psum_tensor(name, shape, F32))

        def sem(name):
            return ctx.enter_context(nc.semaphore(name))

        ids_sb = sb("ids_sb", [TILE, TILES, N_FIELDS], I32)
        ident = sb("ident", [128, 128])
        rows = sb("rows", [TILE, TILES, len(GATHERED), D])
        fields_t = sb("fields_t", [D, BATCH, N])
        dense_sb = sb("dense_sb", [D, BATCH])
        feat = sb("feat", [128, CHUNKS, BATCH])
        wd_a = sb("wd_a", [128, H1])
        wd_b = sb("wd_b", [128, H1])
        wd = sb("wd", [128, H1])
        wp = sb("wp", [128, CHUNKS, H1])
        w2_sb = sb("w2_sb", [128, M1, H2])
        w3_sb = sb("w3_sb", [128, M2])
        b1_sb = sb("b1_sb", [128, M1])
        b2_sb = sb("b2_sb", [128, M2])
        h1 = sb("h1", [128, 2, M1, TILE])
        h2 = sb("h2", [128, 2, M2, TILE])
        y = sb("y", [1, BATCH])
        row_sb = sb("row_sb", [VP, VC])
        bid = sb("bid", [VP, 2, BATCH], I32)
        tab = sb("tab", [VP, 2, VC, D])
        hi = sb("hi", [VP, 2, VC, D], F32R)
        lo = sb("lo", [VP, 2, VC, D], F32R)
        hot = sb("hot", [VP, 2, VC, BATCH], F32R)

        ps_turn = psum("ps_turn", [128, 2, PER_BANK, TILE])
        ps_gram = psum("ps_gram", [128, 2, 2, 512])
        ps_mlp = psum("ps_mlp", [128, 2, 512])

        s_ids = sem("s_ids")
        s_ident = sem("s_ident")
        s_dense = sem("s_dense")
        s_row = sem("s_row")
        s_bid = [sem(f"s_bid{i}") for i in range(2)]
        s_tab = [sem(f"s_tab{i}") for i in range(2)]
        s_w1 = sem("s_w1")
        s_w2 = sem("s_w2")
        s_gather = [[sem(f"s_gather{t}_{g}") for g in range(len(GROUPS))] for t in range(TILES)]
        hi_ready = sem("hi_ready")
        lo_ready = sem("lo_ready")
        hot_ready = sem("hot_ready")
        looked_up = sem("looked_up")
        lookup_copied = sem("lookup_copied")
        dense_placed = sem("dense_placed")
        turned = sem("turned")
        turn_copied_a = sem("turn_copied_a")
        turn_copied_v = sem("turn_copied_v")
        gram_ready = sem("gram_ready")
        spread_a = sem("spread_a")
        spread_v = sem("spread_v")
        wd_ready = sem("wd_ready")
        feat_zeroed = sem("feat_zeroed")
        l1_ready = sem("l1_ready")
        h1_placed = sem("h1_placed")
        l2_ready = sem("l2_ready")
        h2_v = sem("h2_v")
        l3_ready = sem("l3_ready")
        y_ready = sem("y_ready")
        s_out = sem("s_out")

        block = ctx.enter_context(nc.Block())

        @block.sync
        def _(sp):
            sp.dma_start(ids_sb[:], ids).then_inc(s_ids, 16)
            sp.dma_start(row_sb[:], row_of).then_inc(s_row, 16)

            def lookup_loads(k):
                if k >= 2:
                    sp.wait_ge(hot_ready, VC * (k - 1))
                    sp.wait_ge(lo_ready, k - 1)
                sp.dma_start(bid[:, k % 2, :], onehot_ids[k:k + 1, :].broadcast_to((VP, BATCH)))\
                    .then_inc(s_bid[k % 2], 16)
                sp.dma_start(tab[:, k % 2], tables[ONEHOT[k]].rearrange("(p c) d -> p c d", c=VC))\
                    .then_inc(s_tab[k % 2], 16)

            for k in range(min(2, K)):
                lookup_loads(k)
            sp.dma_start(ident[:], ident_in).then_inc(s_ident, 16)
            sp.dma_start(dense_sb[:], dense_t).then_inc(s_dense, 16)
            for k in range(2, min(4, K)):
                lookup_loads(k)
            sp.dma_start(wd_a[:], w_dense_a).then_inc(s_w1, 16)
            sp.dma_start(wd_b[:], w_dense_b).then_inc(s_w1, 16)
            sp.dma_start(wp[:], w_pairs).then_inc(s_w1, 16)
            sp.dma_start(b1_sb[:], b1).then_inc(s_w1, 16)
            sp.dma_start(w2_sb[:], w2).then_inc(s_w2, 16)
            sp.dma_start(w3_sb[:], w3).then_inc(s_w2, 16)
            sp.dma_start(b2_sb[:], b2).then_inc(s_w2, 16)
            for k in range(4, K):
                lookup_loads(k)
            sp.wait_ge(y_ready, TILES)
            sp.dma_start(out, y[:]).then_inc(s_out, 16)
            sp.wait_ge(s_out, 16)

        @block.gpsimd
        def _(pool):
            pool.wait_ge(s_ids, 16)
            for t in range(TILES):
                for n, f in enumerate(GATHERED):
                    pool.indirect_dma_start(
                        out=rows[:, t, n, :], out_offset=None, in_=tables[f][:, :],
                        in_offset=bass.IndirectOffsetOnAxis(ap=ids_sb[:, t, f:f + 1], axis=0))\
                        .then_inc(s_gather[t][n // PER_BANK], 16)

        def turn_copy(copy, eng, t, g, done):
            n = t * len(GROUPS) + g
            eng.wait_ge(turned, n + 1)
            fs = GROUPS[g]
            i = 0
            while i < len(fs):
                w = 1
                while i + w < len(fs) and fs[i + w] == fs[i] + w:
                    w += 1
                dst = fields_t[:, t * TILE:(t + 1) * TILE, fs[i] + 1:fs[i] + 1 + w].rearrange("p b f -> p f b")
                last = copy(dst, ps_turn[:, n % 2, i:i + w, :])
                i += w
            last.then_inc(done, 1)

        def spread(copy, eng, t, u, done):
            n = t * UNITS + u
            eng.wait_ge(gram_ready, n + 1)
            for q in range(4):
                nc_ = -(-(NJ - q) // 4)
                b0 = t * TILE + u * UNIT
                dst = feat[32 * q:32 * q + N, 0:nc_, b0:b0 + UNIT].rearrange("p c (k b) -> p c k b", k=2)
                src = ps_gram[0:N, n % 2, :, 0:GB * NJ].rearrange("p k (b j) -> p j k b", j=NJ)[:, q:NJ:4]
                last = copy(dst, src)
            last.then_inc(done, 1)

        @block.scalar
        def _(act):
            def copy(dst, src):
                return nc.scalar.activation(dst, src, ACT.Copy)

            for k in range(K):
                act.wait_ge(s_tab[k % 2], 16 * (k // 2 + 1))
                if k >= 2:
                    act.wait_ge(looked_up, k - 1)
                copy(hi[:, k % 2], tab[:, k % 2]).then_inc(hi_ready, 1)
                if k >= 1:
                    act.wait_ge(looked_up, k)
                    copy(fields_t[:, :, ONEHOT[k - 1] + 1], ps_mlp[:, (k - 1) % 2, :]).then_inc(lookup_copied, 1)
            if K:
                act.wait_ge(looked_up, K)
                copy(fields_t[:, :, ONEHOT[K - 1] + 1], ps_mlp[:, (K - 1) % 2, :]).then_inc(lookup_copied, 1)
            act.wait_ge(s_w1, 64)
            act.wait_ge(feat_zeroed, 1)

            def relu1(t):
                act.wait_ge(l1_ready, t + 1)
                if t >= 2:
                    act.wait_ge(l2_ready, t - 1)
                for m in range(M1):
                    last = nc.scalar.activation(h1[:, t % 2, m, :], ps_mlp[:, 0, m * TILE:(m + 1) * TILE],
                                                ACT.Relu, bias=b1_sb[:, m:m + 1])
                last.then_inc(h1_placed, 1)

            for t in range(TILES):
                for g in range(1, len(GROUPS), 2):
                    turn_copy(copy, act, t, g, turn_copied_a)
                for u in range(1, UNITS, 2):
                    spread(copy, act, t, u, spread_a)
                relu1(t)

        @block.vector
        def _(dve):
            copy = nc.vector.tensor_copy
            nc.vector.memset(feat[:], 0.0).then_inc(feat_zeroed, 1)
            if K:
                dve.wait_ge(s_row, 16)
            for k in range(K):
                dve.wait_ge(s_bid[k % 2], 16 * (k // 2 + 1))
                if k >= 2:
                    dve.wait_ge(looked_up, k - 1)
                for c in range(VC):
                    nc.vector.tensor_scalar(hot[:, k % 2, c, :], bid[:, k % 2, :], row_sb[:, c:c + 1], None,
                                            ALU.is_equal).then_inc(hot_ready, 1)
                dve.wait_ge(hi_ready, k + 1)
                nc.vector.tensor_tensor(lo[:, k % 2], tab[:, k % 2], hi[:, k % 2].bitcast(F32), ALU.subtract)\
                    .then_inc(lo_ready, 1)
            dve.wait_ge(s_dense, 16)
            copy(fields_t[:, :, 0], dense_sb[:]).then_inc(dense_placed, 1)
            dve.wait_ge(s_w1, 64)
            nc.vector.tensor_tensor(wd[:], wd_a[:], wd_b[:], ALU.add).then_inc(wd_ready, 1)
            dve.wait_ge(feat_zeroed, 1)
            dve.wait_ge(s_w2, 48)

            def relu2(t):
                dve.wait_ge(l2_ready, t + 1)
                if t >= 2:
                    dve.wait_ge(l3_ready, t - 1)
                for m in range(M2):
                    last = nc.vector.tensor_scalar(h2[:, t % 2, m, :], ps_mlp[:, 1, m * TILE:(m + 1) * TILE],
                                                   b2_sb[:, m:m + 1], 0.0, ALU.add, ALU.max)
                last.then_inc(h2_v, 1)

            def y_copy(t):
                dve.wait_ge(l3_ready, t + 1)
                copy(y[:, t * TILE:(t + 1) * TILE], ps_mlp[0:1, 1, M2 * TILE:(M2 + 1) * TILE]).then_inc(y_ready, 1)

            for t in range(TILES):
                for g in range(0, len(GROUPS), 2):
                    turn_copy(copy, dve, t, g, turn_copied_v)
                for u in range(0, UNITS, 2):
                    spread(copy, dve, t, u, spread_v)
                if t >= 1:
                    relu2(t - 1)
                    y_copy(t - 1)
            relu2(TILES - 1)
            y_copy(TILES - 1)

        @block.tensor
        def _(pe):
            for k in range(K):
                if k >= 2:
                    pe.wait_ge(lookup_copied, k - 1)
                pe.wait_ge(hi_ready, k + 1)
                for c in range(VC):
                    pe.wait_ge(hot_ready, VC * k + c + 1)
                    nc.tensor.matmul(ps_mlp[:, k % 2, :], hi[:, k % 2, c, :], hot[:, k % 2, c, :],
                                     start=(c == 0), stop=False)
                pe.wait_ge(lo_ready, k + 1)
                for c in range(VC):
                    last = nc.tensor.matmul(ps_mlp[:, k % 2, :], lo[:, k % 2, c, :], hot[:, k % 2, c, :],
                                            start=False, stop=(c == VC - 1))
                last.then_inc(looked_up, 1)

            NV = -(-len(GROUPS) // 2)
            NA = len(GROUPS) // 2

            def wait_turn(n):
                t, g = divmod(n, len(GROUPS))
                if g % 2:
                    pe.wait_ge(turn_copied_a, t * NA + g // 2 + 1)
                else:
                    pe.wait_ge(turn_copied_v, t * NV + g // 2 + 1)

            def turn(t, g):
                n = t * len(GROUPS) + g
                if n >= 2:
                    wait_turn(n - 2)
                pe.wait_ge(s_gather[t][g], 16 * len(GROUPS[g]))
                for i in range(len(GROUPS[g])):
                    last = nc.tensor.transpose(ps_turn[:, n % 2, i, :], rows[:, t, PER_BANK * g + i, :], ident[:])
                last.then_inc(turned, 1)

            def gram(t, u):
                n = t * UNITS + u
                if n >= 2:
                    pe.wait_ge(spread_a if n % 2 else spread_v, n // 2)
                for s in range(UNIT):
                    b = t * TILE + u * UNIT + s
                    at = (s % GB) * NJ
                    last = nc.tensor.matmul(ps_gram[0:N, n % 2, s // GB, at:at + NJ], fields_t[:, b, :],
                                            fields_t[:, b, 1:N], start=True, stop=True)
                last.then_inc(gram_ready, 1)

            def layer1(t):
                if t == 0:
                    pe.wait_ge(s_w1, 64)
                    pe.wait_ge(wd_ready, 1)
                    if K:
                        pe.wait_ge(lookup_copied, K)
                else:
                    pe.wait_ge(h1_placed, t)
                pe.wait_ge(spread_a, UNITS // 2 * (t + 1))
                pe.wait_ge(spread_v, UNITS // 2 * (t + 1))
                cols = slice(t * TILE, (t + 1) * TILE)
                for m in range(M1):
                    o = ps_mlp[:, 0, m * TILE:(m + 1) * TILE]
                    nc.tensor.matmul(o, wd[:, m:H1:M1], dense_sb[:, cols], start=True, stop=False)
                    for c in range(CHUNKS):
                        p = LAST if c == CHUNKS - 1 else 128
                        last = nc.tensor.matmul(o, wp[0:p, c, m:H1:M1], feat[0:p, c, cols],
                                                start=False, stop=(c == CHUNKS - 1))
                last.then_inc(l1_ready, 1)

            def layers23(t):
                if t == 0:
                    pe.wait_ge(s_w2, 48)
                else:
                    pe.wait_ge(y_ready, t)
                pe.wait_ge(h1_placed, t + 1)
                for n in range(M2):
                    for m in range(M1):
                        last = nc.tensor.matmul(ps_mlp[:, 1, n * TILE:(n + 1) * TILE], w2_sb[:, m, n:H2:M2],
                                                h1[:, t % 2, m, :], start=(m == 0), stop=(m == M1 - 1))
                last.then_inc(l2_ready, 1)
                pe.wait_ge(h2_v, t + 1)
                for n in range(M2):
                    last = nc.tensor.matmul(ps_mlp[0:1, 1, M2 * TILE:(M2 + 1) * TILE], w3_sb[:, n:n + 1],
                                            h2[:, t % 2, n, :], start=(n == 0), stop=(n == M2 - 1))
                last.then_inc(l3_ready, 1)

            pe.wait_ge(s_ident, 16)
            for t in range(TILES):
                for g in range(len(GROUPS)):
                    turn(t, g)
                if t == 0:
                    if K:
                        pe.wait_ge(lookup_copied, K)
                    pe.wait_ge(dense_placed, 1)
                n = (t + 1) * len(GROUPS)
                wait_turn(n - 1)
                wait_turn(n - 2)
                for u in range(UNITS):
                    gram(t, u)
                if t >= 1:
                    layers23(t - 1)
                layer1(t)
            layers23(TILES - 1)


def kernel(**inputs):
    import numpy as np
    import concourse.bacc as bacc
    from concourse.bass_utils import run_bass_kernel_spmd

    w1 = np.asarray(inputs["W_top1"])
    w_pairs = np.zeros((128, CHUNKS, H1), w1.dtype)
    row = D
    for i in range(N):
        for j in range(i + 1, N):
            c, q = divmod(j - 1, 4)
            w_pairs[32 * q + i, c] = w1[row]
            row += 1
    ids = np.asarray(inputs["ids"])
    rows = {
        "dense_t": np.asarray(inputs["r_dense_features"]).T,
        "ids": ids.reshape(TILES, TILE, N_FIELDS).transpose(1, 0, 2),
        "onehot_ids": ids[:, ONEHOT].T if K else ids[:, :1].T,
        "row_of": np.arange(ONEHOT_ROWS, dtype=np.float32).reshape(VP, VC),
        "w_dense_a": w1[:D],
        "w_dense_b": w1[row:],
        "w_pairs": w_pairs,
        "b1": np.asarray(inputs["b_top1"]).reshape(128, M1),
        "w2": np.asarray(inputs["W_top2"]).reshape(128, M1, H2),
        "b2": np.asarray(inputs["b_top2"]).reshape(128, M2),
        "w3": np.asarray(inputs["W_top3"]).reshape(128, M2),
        "ident_in": np.eye(128, dtype=np.float32),
    }
    nc = bacc.Bacc("TRN2", target_bir_lowering=False, num_devices=1)
    arrays = {}

    def dram(name, a):
        arrays[name] = np.ascontiguousarray(a)
        return nc.dram_tensor(name, arrays[name].shape, mybir.dt.from_np(arrays[name].dtype),
                              kind="ExternalInput").ap()

    args = {name: dram(name, a) for name, a in rows.items()}
    tables = [dram(f"tbl_{f}", np.asarray(inputs[f"tbl_{f}"])) for f in range(N_FIELDS)]
    out = nc.dram_tensor("out", (1, BATCH), F32, kind="ExternalOutput").ap()
    tower(nc, tables=tables, out=out, **args)
    result = run_bass_kernel_spmd(nc, [arrays], core_ids=[0])
    return result.results[0]["out"].reshape(BATCH, 1)
```

```python
from contextlib import ExitStack

import concourse.bass as bass
from concourse import mybir

F32 = mybir.dt.float32
F32R = mybir.dt.float32r
I32 = mybir.dt.int32
ALU = mybir.AluOpType
ACT = mybir.ActivationFunctionType

BATCH = 512
D = 128
VOCAB = [1000, 1250, 1250, 125000, 12500, 1000, 1000, 1000, 1250, 12500, 1250, 12500, 12500,
         12500, 1000, 1000, 1250, 12500, 12500, 1250, 12500, 1250, 1250, 1250, 1000, 1000]
N_FIELDS = len(VOCAB)
N = N_FIELDS + 1
NJ = N - 1
LOOKUP_ROWS = 1000
LOOKED_UP = [f for f in range(N_FIELDS) if VOCAB[f] == LOOKUP_ROWS][:7]
K = len(LOOKED_UP)
GATHERED = [f for f in range(N_FIELDS) if f not in LOOKED_UP]
G = len(GATHERED)
SLOTS = [0] + [f + 1 for f in LOOKED_UP + GATHERED]
VC = 8
VP = LOOKUP_ROWS // VC
VC_ACT = 2

UNIT = 32
UNITS = BATCH // UNIT
TILE = 128
TILES = BATCH // TILE
PER_TILE = TILE // UNIT
BLOCKS = 128 // UNIT
GATHERS = UNITS * G // BLOCKS
PER_BANK = 4
BANK_BLOCKS = BLOCKS * PER_BANK
BANKS = -(-GATHERS // PER_BANK)
GB = UNIT // 2
CHUNKS = -(-NJ // 4)
LAST = 32 * (NJ - 4 * (CHUNKS - 1))
H1, H2 = 512, 256
M1, M2 = H1 // 128, H2 // 128


def bank_of(u):
    return (G * (u + 1) - 1) // BANK_BLOCKS


def segments(n):
    at, end = n * BANK_BLOCKS, min((n + 1) * BANK_BLOCKS, UNITS * G)
    while at < end:
        u, f = divmod(at, G)
        w = min(G - f, end - at)
        yield at - n * BANK_BLOCKS, u, f, w
        at += w


def schedule():
    steps, n = [], 0
    for u in range(UNITS):
        ahead = u + 1 if u < UNITS - 2 else u
        while n <= bank_of(ahead):
            steps.append(("turn", n))
            n += 1
        steps.append(("gram", u))
        t, r = divmod(u, PER_TILE)
        if t and r == 0:
            steps.append(("layer1", t - 1))
        if t and r == 1:
            steps.append(("layers23", t - 1))
    return steps


SCHEDULE = schedule()


def tower(nc, dense_t, idx, base, lookup_ids, row_of, minus_row, zeros, store, tables, w_dense_a, w_dense_b,
          w_pairs, b1, w2, b2, w3, identity, out):
    with ExitStack() as ctx:
        def sb(name, shape, dt=F32):
            return ctx.enter_context(nc.sbuf_tensor(name, shape, dt))

        def psum(name, shape):
            return ctx.enter_context(nc.psum_tensor(name, shape, F32))

        def sem(name):
            return ctx.enter_context(nc.semaphore(name))

        idx_raw = sb("idx_raw", [128, GATHERS], I32)
        base_sb = sb("base_sb", [128, GATHERS], I32)
        idx_sb = sb("idx_sb", [128, GATHERS], I32)
        ident = sb("ident", [128, 128])
        rows = sb("rows", [128, GATHERS, D])
        fields_t = sb("fields_t", [D, BATCH, N])
        dense_sb = sb("dense_sb", [D, BATCH])
        feat = sb("feat", [128, CHUNKS, BATCH])
        wd_a = sb("wd_a", [128, H1])
        wd_b = sb("wd_b", [128, H1])
        wd = sb("wd", [128, H1])
        wp = sb("wp", [128, CHUNKS, H1])
        w2_sb = sb("w2_sb", [128, M1, H2])
        w3_sb = sb("w3_sb", [128, M2])
        b1_sb = sb("b1_sb", [128, M1])
        b2_sb = sb("b2_sb", [128, M2])
        h1 = sb("h1", [128, 2, M1, TILE])
        h2 = sb("h2", [128, 2, M2, TILE])
        y = sb("y", [1, BATCH])
        row_sb = sb("row_sb", [VP, VC])
        minus_row_sb = sb("minus_row_sb", [VP, VC])
        bid = sb("bid", [VP, 2, BATCH], I32)
        tab = sb("tab", [VP, 2, VC, D])
        away = sb("away", [VP, VC_ACT, BATCH])
        hi = sb("hi", [VP, 2, VC, D], F32R)
        lo = sb("lo", [VP, 2, VC, D], F32R)
        hot = sb("hot", [VP, 2, VC, BATCH], F32R)

        ps_turn = psum("ps_turn", [128, 2, BANK_BLOCKS, UNIT])
        ps_gram = psum("ps_gram", [128, 2, 2, 512])
        ps_mlp = psum("ps_mlp", [128, 2, 512])

        s_idx = sem("s_idx")
        s_ident = sem("s_ident")
        s_dense = sem("s_dense")
        s_row = sem("s_row")
        s_zeros = sem("s_zeros")
        s_bid = [sem(f"s_bid{i}") for i in range(2)]
        s_tab = [sem(f"s_tab{i}") for i in range(2)]
        s_w1 = sem("s_w1")
        s_w2 = sem("s_w2")
        s_gather = [sem(f"s_gather{n}") for n in range(BANKS)]
        idx_ready = sem("idx_ready")
        hi_ready = sem("hi_ready")
        lo_ready = sem("lo_ready")
        away_ready = sem("away_ready")
        hot_a = sem("hot_a")
        hot_v = sem("hot_v")
        looked_up = sem("looked_up")
        lookup_copied = sem("lookup_copied")
        dense_placed = sem("dense_placed")
        turned = sem("turned")
        turn_copied = [sem("turn_copied_v"), sem("turn_copied_a")]
        gram_ready = sem("gram_ready")
        spread = [sem("spread_v"), sem("spread_a")]
        wd_ready = sem("wd_ready")
        l1_ready = sem("l1_ready")
        h1_placed = sem("h1_placed")
        h1_last = [sem("h1_last_v"), sem("h1_last_a")]
        l2_ready = sem("l2_ready")
        h2_placed = sem("h2_placed")
        h2_last = [sem("h2_last_v"), sem("h2_last_a")]
        l3_ready = sem("l3_ready")
        y_ready = sem("y_ready")
        s_out = sem("s_out")

        block = ctx.enter_context(nc.Block())

        @block.sync
        def _(sp):
            sp.dma_start(idx_raw[:], idx).then_inc(s_idx, 16)
            sp.dma_start(row_sb[:], row_of).then_inc(s_row, 16)

            def lookup_loads(k):
                if k >= 2:
                    sp.wait_ge(hot_v, (VC - VC_ACT) * (k - 1))
                    sp.wait_ge(away_ready, VC_ACT * (k - 1))
                sp.dma_start(bid[:, k % 2, :], lookup_ids[k:k + 1, :].broadcast_to((VP, BATCH)))\
                    .then_inc(s_bid[k % 2], 16)
                if k >= 2:
                    sp.wait_ge(lo_ready, k - 1)
                src = tables[k].rearrange("(p c) d -> p c d", c=VC)
                for p0, p1 in ((0, VP // 16 * 16), (VP // 16 * 16, VP)):
                    sp.dma_start(tab[p0:p1, k % 2], src[p0:p1]).then_inc(s_tab[k % 2], 16)

            lookup_loads(0)
            sp.dma_start(dense_sb[:], dense_t).then_inc(s_dense, 16)
            for k in range(1, K):
                lookup_loads(k)
                if k == 2:
                    sp.dma_start(ident[:], identity).then_inc(s_ident, 16)
                    sp.dma_start(wd_a[:], w_dense_a).then_inc(s_w1, 16)
                    sp.dma_start(wd_b[:], w_dense_b).then_inc(s_w1, 16)
                    sp.dma_start(b1_sb[:], b1).then_inc(s_w1, 16)
            sp.dma_start(wp[:], w_pairs).then_inc(s_w1, 16)
            for q in range(4):
                sp.dma_start(feat[32 * q + N:32 * q + 32, :, :], zeros).then_inc(s_zeros, 16)
            sp.dma_start(w2_sb[:], w2).then_inc(s_w2, 16)
            sp.dma_start(w3_sb[:], w3).then_inc(s_w2, 16)
            sp.dma_start(b2_sb[:], b2).then_inc(s_w2, 16)
            sp.wait_ge(y_ready, TILES)
            sp.dma_start(out, y[:]).then_inc(s_out, 16)
            sp.wait_ge(s_out, 16)

        @block.gpsimd
        def _(pool):
            pool.wait_ge(idx_ready, 1)
            for m in range(GATHERS):
                pool.indirect_dma_start(out=rows[:, m, :], out_offset=None, in_=store[:, :],
                                        in_offset=bass.IndirectOffsetOnAxis(ap=idx_sb[:, m:m + 1], axis=0))\
                    .then_inc(s_gather[m // PER_BANK], 16)

        def copy_turned(eng, copy, n):
            eng.wait_ge(turned, n + 1)
            for i, u, f, w in segments(n):
                dst = fields_t[:, u * UNIT:(u + 1) * UNIT, 1 + K + f:1 + K + f + w].rearrange("p b f -> p f b")
                last = copy(dst, ps_turn[:, n % 2, i:i + w, :])
            last.then_inc(turn_copied[n % 2], 1)

        def spread_grams(eng, copy, u):
            eng.wait_ge(gram_ready, u + 1)
            for q in range(4):
                full = -(-(NJ - q) // 4)
                dst = feat[32 * q:32 * q + N, 0:full, u * UNIT:(u + 1) * UNIT].rearrange("p c (k b) -> p c k b", k=2)
                src = ps_gram[0:N, u % 2, :, 0:GB * NJ].rearrange("p k (b j) -> p j k b", j=NJ)[:, q:NJ:4]
                last = copy(dst, src)
            last.then_inc(spread[u % 2], 1)

        @block.scalar
        def _(act):
            def copy(dst, src):
                return nc.scalar.activation(dst, src, ACT.Copy)

            act.dma_start(base_sb[:], base).then_inc(s_idx, 16)
            act.dma_start(minus_row_sb[:], minus_row).then_inc(s_row, 16)
            act.wait_ge(s_row, 32)
            for k in range(K + 1):
                if k < K:
                    act.wait_ge(s_bid[k % 2], 16 * (k // 2 + 1))
                    if k >= 1:
                        act.wait_ge(hot_a, VC_ACT * k)
                    for c in range(VC_ACT):
                        nc.scalar.activation(away[:, c, :], bid[:, k % 2, :], ACT.Abs,
                                             bias=minus_row_sb[:, c:c + 1]).then_inc(away_ready, 1)
                    act.wait_ge(s_tab[k % 2], 32 * (k // 2 + 1))
                    if k >= 2:
                        act.wait_ge(looked_up, k - 1)
                    copy(hi[:, k % 2], tab[:, k % 2]).then_inc(hi_ready, 1)
                    for c in range(VC_ACT):
                        act.wait_ge(away_ready, VC_ACT * k + c + 1)
                        nc.scalar.activation(hot[:, k % 2, c, :], away[:, c, :], ACT.Relu, bias=1.0,
                                             scale=-1.0).then_inc(hot_a, 1)
                if k == 0:
                    act.wait_ge(s_dense, 16)
                    copy(fields_t[:, :, 0], dense_sb[:]).then_inc(dense_placed, 1)
                else:
                    act.wait_ge(looked_up, k)
                    copy(fields_t[:, :, k], ps_mlp[:, (k - 1) % 2, :]).then_inc(lookup_copied, 1)
            act.wait_ge(s_w1, 64)
            act.wait_ge(s_w2, 48)

            def relu1(t):
                act.wait_ge(l1_ready, t + 1)
                if t >= 2:
                    act.wait_ge(l2_ready, t - 1)
                for m in range(M1):
                    last = nc.scalar.activation(h1[:, t % 2, m, :], ps_mlp[:, 0, m * TILE:(m + 1) * TILE],
                                                ACT.Relu, bias=b1_sb[:, m:m + 1])
                last.then_inc(h1_placed, 1)

            for step, n in SCHEDULE:
                if step == "turn" and n % 2 == 1:
                    copy_turned(act, copy, n)
                if step == "gram" and n % 2 == 1:
                    spread_grams(act, copy, n)
                if step == "layer1":
                    relu1(n)
            t = TILES - 1
            for m in range(1, M1, 2):
                act.wait_ge(l1_ready, t + m + 1)
                nc.scalar.activation(h1[:, t % 2, m, :], ps_gram[:, m // 2, m % 2, 0:TILE],
                                     ACT.Relu, bias=b1_sb[:, m:m + 1]).then_inc(h1_last[1], 1)
            act.wait_ge(l2_ready, t + 2)
            nc.scalar.activation(h2[:, t % 2, 1, :], ps_mlp[:, 0, 0:TILE], ACT.Relu, bias=b2_sb[:, 1:2])\
                .then_inc(h2_last[1], 1)

        @block.vector
        def _(dve):
            copy = nc.vector.tensor_copy
            dve.wait_ge(s_idx, 32)
            nc.vector.tensor_tensor(idx_sb[:], idx_raw[:], base_sb[:], ALU.add).then_inc(idx_ready, 1)
            dve.wait_ge(s_row, 32)
            for k in range(K):
                dve.wait_ge(s_bid[k % 2], 16 * (k // 2 + 1))
                if k >= 2:
                    dve.wait_ge(looked_up, k - 1)
                for c in range(VC_ACT, VC):
                    nc.vector.tensor_scalar(hot[:, k % 2, c, :], bid[:, k % 2, :], row_sb[:, c:c + 1], None,
                                            ALU.is_equal).then_inc(hot_v, 1)
                dve.wait_ge(hi_ready, k + 1)
                nc.vector.tensor_tensor(lo[:, k % 2], tab[:, k % 2], hi[:, k % 2].bitcast(F32), ALU.subtract)\
                    .then_inc(lo_ready, 1)
            dve.wait_ge(s_w1, 64)
            dve.wait_ge(s_w2, 48)

            def relu2(t):
                dve.wait_ge(l2_ready, t + 1)
                if t >= 2:
                    dve.wait_ge(l3_ready, t - 1)
                for m in range(M2):
                    last = nc.vector.tensor_scalar(h2[:, t % 2, m, :], ps_mlp[:, 1, m * TILE:(m + 1) * TILE],
                                                   b2_sb[:, m:m + 1], 0.0, ALU.add, ALU.max)
                last.then_inc(h2_placed, 1)

            for step, n in SCHEDULE:
                if step == "turn" and n % 2 == 0:
                    copy_turned(dve, copy, n)
                if step == "turn" and n == 2:
                    nc.vector.tensor_tensor(wd[:], wd_a[:], wd_b[:], ALU.add).then_inc(wd_ready, 1)
                if step == "gram" and n % 2 == 0:
                    spread_grams(dve, copy, n)
                if step == "layers23":
                    relu2(n)
                    dve.wait_ge(l3_ready, n + 1)
                    copy(y[:, n * TILE:(n + 1) * TILE], ps_mlp[0:1, 1, M2 * TILE:(M2 + 1) * TILE])\
                        .then_inc(y_ready, 1)
            t = TILES - 1
            for m in range(0, M1, 2):
                dve.wait_ge(l1_ready, t + m + 1)
                nc.vector.tensor_scalar(h1[:, t % 2, m, :], ps_gram[:, m // 2, m % 2, 0:TILE],
                                        b1_sb[:, m:m + 1], 0.0, ALU.add, ALU.max).then_inc(h1_last[0], 1)
            dve.wait_ge(l2_ready, t + 1)
            nc.vector.tensor_scalar(h2[:, t % 2, 0, :], ps_mlp[:, 1, 0:TILE], b2_sb[:, 0:1], 0.0,
                                    ALU.add, ALU.max).then_inc(h2_last[0], 1)
            dve.wait_ge(l3_ready, t + 1)
            copy(y[:, t * TILE:], ps_turn[0:1, 0, 0:TILE // UNIT, :].rearrange("p f b -> p (f b)"))\
                .then_inc(y_ready, 1)

        @block.tensor
        def _(pe):
            for k in range(K):
                if k >= 2:
                    pe.wait_ge(lookup_copied, k - 1)
                pe.wait_ge(hi_ready, k + 1)
                for n, c in enumerate([*range(VC_ACT, VC), *range(VC_ACT)]):
                    if c < VC_ACT:
                        pe.wait_ge(hot_a, VC_ACT * k + c + 1)
                    else:
                        pe.wait_ge(hot_v, (VC - VC_ACT) * k + c - VC_ACT + 1)
                    nc.tensor.matmul(ps_mlp[:, k % 2, :], hi[:, k % 2, c, :], hot[:, k % 2, c, :],
                                     start=(n == 0), stop=False)
                pe.wait_ge(lo_ready, k + 1)
                for c in range(VC):
                    last = nc.tensor.matmul(ps_mlp[:, k % 2, :], lo[:, k % 2, c, :], hot[:, k % 2, c, :],
                                            start=False, stop=(c == VC - 1))
                last.then_inc(looked_up, 1)

            def copied(n):
                pe.wait_ge(turn_copied[n % 2], n // 2 + 1)

            def turn(n):
                if n >= 2:
                    copied(n - 2)
                gathers = range(n * PER_BANK, min((n + 1) * PER_BANK, GATHERS))
                pe.wait_ge(s_gather[n], 16 * len(gathers))
                for m in gathers:
                    i = BLOCKS * (m % PER_BANK)
                    last = nc.tensor.transpose(ps_turn[:, n % 2, i:i + BLOCKS, :], rows[:, m, :], ident[:])
                last.then_inc(turned, 1)

            def gram(u):
                if u == 0:
                    pe.wait_ge(lookup_copied, K)
                    pe.wait_ge(dense_placed, 1)
                if u >= 2:
                    pe.wait_ge(spread[u % 2], u // 2)
                copied(bank_of(u))
                if bank_of(u):
                    copied(bank_of(u) - 1)
                for s in range(UNIT):
                    at = (s % GB) * NJ
                    last = nc.tensor.matmul(ps_gram[0:N, u % 2, s // GB, at:at + NJ], fields_t[:, u * UNIT + s, :],
                                            fields_t[:, u * UNIT + s, 1:N], start=True, stop=True)
                last.then_inc(gram_ready, 1)

            def layer1(t, m, o):
                cols = slice(t * TILE, (t + 1) * TILE)
                nc.tensor.matmul(o, wd[:, m:H1:M1], dense_sb[:, cols], start=True, stop=False)
                for c in range(CHUNKS):
                    p = LAST if c == CHUNKS - 1 else 128
                    last = nc.tensor.matmul(o, wp[0:p, c, m:H1:M1], feat[0:p, c, cols],
                                            start=False, stop=(c == CHUNKS - 1))
                return last

            def features(t):
                if t == 0:
                    pe.wait_ge(s_w1, 64)
                    pe.wait_ge(wd_ready, 1)
                    pe.wait_ge(s_zeros, 64)
                for e in range(2):
                    pe.wait_ge(spread[e], PER_TILE // 2 * (t + 1))

            def layers23(t):
                if t == 0:
                    pe.wait_ge(s_w2, 48)
                else:
                    pe.wait_ge(y_ready, t)
                pe.wait_ge(h1_placed, t + 1)
                for n in range(M2):
                    for m in range(M1):
                        last = nc.tensor.matmul(ps_mlp[:, 1, n * TILE:(n + 1) * TILE], w2_sb[:, m, n:H2:M2],
                                                h1[:, t % 2, m, :], start=(m == 0), stop=(m == M1 - 1))
                last.then_inc(l2_ready, 1)
                pe.wait_ge(h2_placed, t + 1)
                for n in range(M2):
                    last = nc.tensor.matmul(ps_mlp[0:1, 1, M2 * TILE:(M2 + 1) * TILE], w3_sb[:, n:n + 1],
                                            h2[:, t % 2, n, :], start=(n == 0), stop=(n == M2 - 1))
                last.then_inc(l3_ready, 1)

            pe.wait_ge(s_ident, 16)
            for step, n in SCHEDULE:
                if step == "turn":
                    turn(n)
                if step == "gram":
                    gram(n)
                if step == "layer1":
                    if n:
                        pe.wait_ge(h1_placed, n)
                    features(n)
                    for m in range(M1):
                        last = layer1(n, m, ps_mlp[:, 0, m * TILE:(m + 1) * TILE])
                    last.then_inc(l1_ready, 1)
                if step == "layers23":
                    layers23(n)

            t = TILES - 1
            features(t)
            for m in range(M1):
                layer1(t, m, ps_gram[:, m // 2, m % 2, 0:TILE]).then_inc(l1_ready, 1)
            pe.wait_ge(y_ready, t)
            pe.wait_ge(h1_placed, t)
            for m in range(M1):
                pe.wait_ge(h1_last[m % 2], m // 2 + 1)
                for n in range(M2):
                    last = nc.tensor.matmul(ps_mlp[:, 1 - n, 0:TILE], w2_sb[:, m, n:H2:M2], h1[:, t % 2, m, :],
                                            start=(m == 0), stop=(m == M1 - 1))
                    if m == M1 - 1:
                        last.then_inc(l2_ready, 1)
            for n in range(M2):
                pe.wait_ge(h2_last[n], 1)
                last = nc.tensor.matmul(ps_turn[0:1, 0, 0:TILE // UNIT, :], w3_sb[:, n:n + 1], h2[:, t % 2, n, :],
                                        start=(n == 0), stop=(n == M2 - 1))
            last.then_inc(l3_ready, 1)


def kernel(**inputs):
    import numpy as np
    import concourse.bacc as bacc
    from concourse.bass_utils import run_bass_kernel_spmd

    tables = [np.asarray(inputs[f"tbl_{f}"]) for f in range(N_FIELDS)]
    w1 = np.asarray(inputs["W_top1"])
    w_pairs = np.zeros((128, CHUNKS, H1), w1.dtype)
    first = np.cumsum([D] + [N - 1 - i for i in range(N)])
    for a in range(N):
        for b in range(a + 1, N):
            i, j = sorted((SLOTS[a], SLOTS[b]))
            c, q = divmod(b - 1, 4)
            w_pairs[32 * q + a, c] = w1[first[i] + j - i - 1]
    ids = np.asarray(inputs["ids"])
    begins = np.cumsum([0] + [VOCAB[f] for f in GATHERED[:-1]]).astype(np.int32)

    def gather_order(a):
        return a.reshape(UNITS, UNIT, G).transpose(0, 2, 1).reshape(GATHERS, 128).T

    row = np.arange(LOOKUP_ROWS, dtype=np.float32).reshape(VP, VC)
    arranged = {
        "dense_t": np.asarray(inputs["r_dense_features"]).T,
        "idx": gather_order(ids[:, GATHERED]),
        "base": gather_order(np.broadcast_to(begins, (BATCH, G))),
        "lookup_ids": ids[:, LOOKED_UP].T,
        "row_of": row,
        "minus_row": -row,
        "zeros": np.zeros((32 - N, CHUNKS, BATCH), np.float32),
        "store": np.concatenate([tables[f] for f in GATHERED]),
        "w_dense_a": w1[:D],
        "w_dense_b": w1[-D:],
        "w_pairs": w_pairs,
        "b1": np.asarray(inputs["b_top1"]).reshape(128, M1),
        "w2": np.asarray(inputs["W_top2"]).reshape(128, M1, H2),
        "b2": np.asarray(inputs["b_top2"]).reshape(128, M2),
        "w3": np.asarray(inputs["W_top3"]).reshape(128, M2),
        "identity": np.eye(128, dtype=np.float32),
    }
    nc = bacc.Bacc("TRN2", target_bir_lowering=False, num_devices=1)
    arrays = {}

    def dram(name, a):
        arrays[name] = np.ascontiguousarray(a)
        return nc.dram_tensor(name, arrays[name].shape, mybir.dt.from_np(arrays[name].dtype),
                              kind="ExternalInput").ap()

    args = {name: dram(name, a) for name, a in arranged.items()}
    lookups = [dram(f"tbl_{f}", tables[f]) for f in LOOKED_UP]
    out = nc.dram_tensor("out", (1, BATCH), F32, kind="ExternalOutput").ap()
    tower(nc, tables=lookups, out=out, **args)
    result = run_bass_kernel_spmd(nc, [arrays], core_ids=[0])
    return result.results[0]["out"].reshape(BATCH, 1)
```

```python
from contextlib import ExitStack

import concourse.bass as bass
from concourse import mybir

F32 = mybir.dt.float32
F32R = mybir.dt.float32r
I32 = mybir.dt.int32
ALU = mybir.AluOpType
ACT = mybir.ActivationFunctionType

BATCH = 512
D = 128
VOCAB = [1000, 1250, 1250, 125000, 12500, 1000, 1000, 1000, 1250, 12500, 1250, 12500, 12500,
         12500, 1000, 1000, 1250, 12500, 12500, 1250, 12500, 1250, 1250, 1250, 1000, 1000]
N_FIELDS = len(VOCAB)
N = N_FIELDS + 1
NJ = N - 1
LOOKUP_ROWS = 1000
LOOKED_UP = [f for f in range(N_FIELDS) if VOCAB[f] == LOOKUP_ROWS][:8]
K = len(LOOKED_UP)
GATHERED = [f for f in range(N_FIELDS) if f not in LOOKED_UP]
G = len(GATHERED)
SLOTS = [0] + [f + 1 for f in LOOKED_UP + GATHERED]
VC = 8
VP = LOOKUP_ROWS // VC
LOADS = 3
VC_ACT = 2

UNIT = 32
UNITS = BATCH // UNIT
TILE = 128
TILES = BATCH // TILE
PER_TILE = TILE // UNIT
BLOCKS = 128 // UNIT
GATHERS = UNITS * G // BLOCKS
PER_BANK = 4
LAST_BANK = (GATHERS - 1) // PER_BANK * PER_BANK
BANK_BLOCKS = BLOCKS * PER_BANK
BANKS = -(-GATHERS // PER_BANK)
GB = UNIT // 2
CHUNKS = 3
QS = 4
SHORT = QS * CHUNKS
LONG = NJ - SHORT
PARTS = [(1, 6, 26, 0, 3, 24, 0), (2, 9, 23, 0, 3, 21, 0), (0, 3, 20, 0, 3, 18, 0), (3, 12, 20, 0, 3, 15, 0),
         (0, 23, 9, 0, 2, 13, 0), (0, 23, 4, 2, 1, 13, 9), (0, 27, 5, 2, 1, 14, 9)]
H1, H2 = 512, 256
M1, M2 = H1 // 128, H2 // 128


def bank_of(u):
    return (G * (u + 1) - 1) // BANK_BLOCKS


def segments(n):
    at, end = n * BANK_BLOCKS, min((n + 1) * BANK_BLOCKS, UNITS * G)
    while at < end:
        u, f = divmod(at, G)
        w = min(G - f, end - at)
        yield at - n * BANK_BLOCKS, u, f, w
        at += w


def spread_count(t, e):
    return PER_TILE // 2 * (t + 1) + (e == 0 and t == TILES - 1)


ORDER = """
t0 t1 t2 g0 t3 t4 g1 t5 g2 g3 t6 t7 g4 g5 t8 g6 g7 t9 t10 a0/0 a0/1 g8 t11 a0/2 a0/3 g9 t12 b0
a1/0 t13 a1/1 a1/2 g10 c0 t14 a1/3 g11 t15 b1 g12 c1 t16 g13 g14 t17 a2/0 g15 a2/1 a2/2 a2/3 d3 b2
a3/0 a3/1 a3/2 a3/3 c2
"""
STEPS = {"d": "dense", "t": "turn", "g": "gram", "a": "layer1", "b": "layer2", "c": "layer3"}
SCHEDULE = [(STEPS[x[0]], *map(int, x[1:].split("/")), 0)[:3] for x in ORDER.split()]
POOL_PARTS = 3
EARLY_TURNS = (5, 6)
WD_AFTER = 9


def tower(nc, dense_t, idx, lookup_ids, store, tables, w_dense_a, w_dense_b,
          w_folded, b1, w2, b2, w3, identity, out):
    with ExitStack() as ctx:
        def sb(name, shape, dt=F32):
            return ctx.enter_context(nc.sbuf_tensor(name, shape, dt))

        def psum(name, shape):
            return ctx.enter_context(nc.psum_tensor(name, shape, F32))

        def sem(name):
            return ctx.enter_context(nc.semaphore(name))

        idx_parts = sb("idx_parts", [128, 2 * GATHERS + VC], I32)
        idx_sb = sb("idx_sb", [128, GATHERS], I32)
        ident = sb("ident", [128, 128])
        rows = sb("rows", [128, GATHERS, D])
        fields_t = sb("fields_t", [D, BATCH, N])
        dense_sb = sb("dense_sb", [D, BATCH])
        folded = sb("folded", [128, CHUNKS, BATCH])
        wd = sb("wd", [128, H1])
        wd_b = sb("wd_b", [128, H1])
        w_folded_sb = sb("w_folded_sb", [128, CHUNKS, H1])
        w2_sb = sb("w2_sb", [128, M1, H2])
        w3_sb = sb("w3_sb", [128, M2])
        b1_sb = sb("b1_sb", [128, M1])
        b2_sb = sb("b2_sb", [128, M2])
        row_sb = sb("row_sb", [VP, 2 * VC])
        with ExitStack() as lookups:
            def early(name, shape, dt=F32):
                return lookups.enter_context(nc.sbuf_tensor(name, shape, dt))

            bid = early("bid", [VP, LOADS, BATCH], I32)
            tab = early("tab", [VP, LOADS, VC, D])
            away = early("away", [VP, VC_ACT, BATCH])
            hi = early("hi", [VP, 2, VC, D], F32R)
            lo = early("lo", [VP, 2, VC, D], F32R)
            hot = early("hot", [VP, 2, VC, BATCH], F32R)
        stage = sb("stage", [N, 2, LONG, TILE])
        h1 = sb("h1", [128, 2, M1, TILE])
        h2 = sb("h2", [128, 2, M2, TILE])
        y = sb("y", [1, BATCH])

        ps_turn = psum("ps_turn", [128, 2, BANK_BLOCKS, UNIT])
        ps_gram = psum("ps_gram", [128, 2, 2, 512])
        ps_mlp = psum("ps_mlp", [128, 2, 512])

        s_idx = sem("s_idx")
        s_ident = sem("s_ident")
        s_dense = sem("s_dense")
        s_bid = [sem(f"s_bid{i}") for i in range(LOADS)]
        s_tab = [sem(f"s_tab{i}") for i in range(LOADS)]
        s_w1 = sem("s_w1")
        s_w2 = sem("s_w2")
        s_gather = [sem(f"s_gather{n}") for n in range(BANKS - 1)]
        s_last_gather = [sem(f"s_last_gather{i}") for i in range(GATHERS - LAST_BANK)]
        idx_ready = sem("idx_ready")
        row_ready = sem("row_ready")
        hi_ready = sem("hi_ready")
        lo_ready = sem("lo_ready")
        away_ready = sem("away_ready")
        hot_a = sem("hot_a")
        hot_v = sem("hot_v")
        looked_up = sem("looked_up")
        lookup_copied = sem("lookup_copied")
        dense_placed = sem("dense_placed")
        turned = sem("turned")
        turn_copied = [sem("turn_copied_v"), sem("turn_copied_a")]
        gram_ready = sem("gram_ready")
        staged = [sem("staged_v"), sem("staged_a")]
        spread = [sem("spread_v"), sem("spread_a")]
        s_fold = [sem(f"s_fold{t}") for t in range(TILES)]
        s_fold_pool = sem("s_fold_pool")
        wd_ready = sem("wd_ready")
        l1_ready = sem("l1_ready")
        h1_placed = sem("h1_placed")
        h1_last = [sem("h1_last_v"), sem("h1_last_a")]
        l2_ready = sem("l2_ready")
        h2_placed = sem("h2_placed")
        h2_last = [sem("h2_last_v"), sem("h2_last_a")]
        l3_ready = sem("l3_ready")
        y_ready = sem("y_ready")
        s_out = sem("s_out")

        block = ctx.enter_context(nc.Block())

        def fold(eng, t, parts, folded_parts):
            for e in range(2):
                eng.wait_ge(staged[e], spread_count(t, e))
            for q, row, n, c, cs, j, i in parts:
                eng.dma_start(folded[32 * q + row:32 * q + row + n, c:c + cs, t * TILE:(t + 1) * TILE],
                              stage[i:i + n, t % 2, j - SHORT - 1:j - SHORT - 1 + cs, :])\
                    .then_inc(folded_parts, 16)

        @block.sync
        def _(sp):
            def lookup_loads(k):
                b = k % LOADS
                if k >= LOADS:
                    sp.wait_ge(hot_v, (VC - VC_ACT) * (k - LOADS + 1))
                    sp.wait_ge(away_ready, VC_ACT * (k - LOADS + 1))
                    sp.wait_ge(lo_ready, k - LOADS + 1)
                sp.dma_start(bid[:, b, :], lookup_ids[k:k + 1, :].broadcast_to((VP, BATCH))).then_inc(s_bid[b], 16)
                src = tables[k].rearrange("(p c) d -> p c d", c=VC)
                for p0, p1 in ((0, VP // 16 * 16), (VP // 16 * 16, VP)):
                    sp.dma_start(tab[p0:p1, b], src[p0:p1]).then_inc(s_tab[b], 16)

            sp.dma_start(idx_parts[:], idx).then_inc(s_idx, 16)
            for k in range(K):
                lookup_loads(k)
                if k == 2:
                    sp.dma_start(dense_sb[:], dense_t).then_inc(s_dense, 16)
                    sp.dma_start(ident[:], identity).then_inc(s_ident, 16)
            sp.dma_start(wd[:], w_dense_a).then_inc(s_w1, 16)
            sp.dma_start(wd_b[:], w_dense_b).then_inc(s_w1, 16)
            sp.dma_start(b1_sb[:], b1).then_inc(s_w1, 16)
            sp.dma_start(w_folded_sb[:], w_folded).then_inc(s_w1, 16)
            sp.dma_start(w2_sb[:], w2).then_inc(s_w2, 16)
            sp.dma_start(w3_sb[:], w3).then_inc(s_w2, 16)
            sp.dma_start(b2_sb[:], b2).then_inc(s_w2, 16)
            for t in range(TILES):
                fold(sp, t, PARTS[POOL_PARTS:] if t == TILES - 1 else PARTS, s_fold[t])
            sp.wait_ge(y_ready, TILES)
            sp.dma_start(out, y[:]).then_inc(s_out, 16)
            sp.wait_ge(s_out, 16)

        @block.gpsimd
        def _(pool):
            pool.wait_ge(idx_ready, 1)
            for m in range(GATHERS):
                pool.indirect_dma_start(out=rows[:, m, :], out_offset=None, in_=store[:, :],
                                        in_offset=bass.IndirectOffsetOnAxis(ap=idx_sb[:, m:m + 1], axis=0))\
                    .then_inc(s_gather[m // PER_BANK] if m < LAST_BANK else s_last_gather[m - LAST_BANK], 16)
            fold(pool, TILES - 1, PARTS[:POOL_PARTS], s_fold_pool)

        def copy_turned(eng, copy, n):
            eng.wait_ge(turned, n + 1)
            for i, u, f, w in segments(n):
                dst = fields_t[:, u * UNIT:(u + 1) * UNIT, 1 + K + f:1 + K + f + w].rearrange("p b f -> p f b")
                last = copy(dst, ps_turn[:, n % 2, i:i + w, :])
            last.then_inc(turn_copied[n % 2], 1)

        def spread_grams(eng, copy, u, k0=0, k1=2):
            eng.wait_ge(gram_ready, u + (k1 if u == UNITS - 1 else 1))
            t, at = u // PER_TILE, u % PER_TILE * UNIT
            grams = ps_gram[0:N, u % 2, k0:k1, 0:GB * NJ].rearrange("p k (b j) -> p j k b", j=NJ)
            b0, b1, ks = k0 * GB, k1 * GB, k1 - k0
            if t >= 2:
                eng.wait_ge(s_fold[t - 2], 16 * len(PARTS))
            e = k0 if u == UNITS - 1 else u % 2
            copy(stage[:, t % 2, :, at + b0:at + b1].rearrange("p j (k b) -> p j k b", k=ks), grams[:, SHORT:])\
                .then_inc(staged[e], 1)
            for q in range(QS):
                rows_q = CHUNKS * (q + 1)
                dst = folded[32 * q:32 * q + rows_q, :, u * UNIT + b0:u * UNIT + b1]
                last = copy(dst.rearrange("p c (k b) -> p c k b", k=ks),
                            grams[0:rows_q, CHUNKS * q:CHUNKS * (q + 1)])
            last.then_inc(spread[e], 1)

        @block.scalar
        def _(act):
            def copy(dst, src):
                return nc.scalar.activation(dst, src, ACT.Copy)

            act.wait_ge(s_idx, 16)
            for i, sign in enumerate((1.0, -1.0)):
                nc.scalar.activation(row_sb[:, i * VC:(i + 1) * VC], idx_parts[0:VP, 2 * GATHERS:], ACT.Copy,
                                     scale=sign).then_inc(row_ready, 1)

            def split(k):
                act.wait_ge(s_tab[k % LOADS], 32 * (k // LOADS + 1))
                if k >= 2:
                    act.wait_ge(looked_up, k - 1)
                halves = 2 if k == 0 else 1
                for c in range(0, VC, VC // halves):
                    copy(hi[:, k % 2, c:c + VC // halves], tab[:, k % LOADS, c:c + VC // halves])\
                        .then_inc(hi_ready, 1)

            act.wait_ge(row_ready, 2)
            for k in range(K + 1):
                if k < K:
                    act.wait_ge(s_bid[k % LOADS], 16 * (k // LOADS + 1))
                    if k >= 1:
                        act.wait_ge(hot_a, k)
                    c0 = VC - VC_ACT
                    for c in range(c0, VC):
                        nc.scalar.activation(away[:, c - c0, :], bid[:, k % LOADS, :], ACT.Abs,
                                             bias=row_sb[:, VC + c:VC + c + 1]).then_inc(away_ready, 1)
                    split(k)
                    act.wait_ge(away_ready, VC_ACT * (k + 1))
                    nc.scalar.activation(hot[:, k % 2, c0:VC, :], away[:, 0:VC - c0, :], ACT.Relu,
                                         bias=1.0, scale=-1.0).then_inc(hot_a, 1)
                if k == K:
                    copy_turned(act, copy, 1)
                if k:
                    act.wait_ge(looked_up, k)
                    copy(fields_t[:, :, k], ps_mlp[:, (k - 1) % 2, :]).then_inc(lookup_copied, 1)

            def relu1(t):
                if t == 0:
                    act.wait_ge(s_w1, 64)
                    act.wait_ge(s_w2, 48)
                act.wait_ge(l1_ready, t + 1)
                if t >= 2:
                    act.wait_ge(l2_ready, t - 1)
                for m in range(M1):
                    nc.scalar.activation(h1[:, t % 2, m, :], ps_mlp[:, 0, m * TILE:(m + 1) * TILE],
                                         ACT.Relu, bias=b1_sb[:, m:m + 1]).then_inc(h1_placed, 1)

            for step, n, m in SCHEDULE:
                if step == "turn" and n % 2 == 1 and n > 1:
                    copy_turned(act, copy, n)
                if step == "gram" and n % 2 == 1:
                    spread_grams(act, copy, n, int(n == UNITS - 1))
                if step == "layer1" and n < TILES - 1 and m == M1 - 1:
                    relu1(n)
                if step == "layer1" and n == TILES - 1 and m % 2 == 1:
                    act.wait_ge(l1_ready, n + m + 1)
                    nc.scalar.activation(h1[:, n % 2, m, :], ps_gram[:, m // 2, m % 2, 0:TILE],
                                         ACT.Relu, bias=b1_sb[:, m:m + 1]).then_inc(h1_last[1], 1)
            t = TILES - 1
            act.wait_ge(l2_ready, t + 2)
            nc.scalar.activation(h2[:, t % 2, 1, :], ps_turn[:, 1, 0:TILE // UNIT, :].rearrange("p f b -> p (f b)"),
                                 ACT.Relu, bias=b2_sb[:, 1:2]).then_inc(h2_last[1], 1)

        @block.vector
        def _(dve):
            copy = nc.vector.tensor_copy
            dve.wait_ge(s_idx, 16)
            nc.vector.tensor_tensor(idx_sb[:], idx_parts[:, 0:GATHERS], idx_parts[:, GATHERS:2 * GATHERS], ALU.add)\
                .then_inc(idx_ready, 1)
            dve.wait_ge(row_ready, 1)
            for k in range(K):
                dve.wait_ge(s_bid[k % LOADS], 16 * (k // LOADS + 1))
                if k >= 2:
                    dve.wait_ge(looked_up, k - 1)
                for c in range(VC - VC_ACT):
                    nc.vector.tensor_scalar(hot[:, k % 2, c, :], bid[:, k % LOADS, :], row_sb[:, c:c + 1], None,
                                            ALU.is_equal).then_inc(hot_v, 1)
                dve.wait_ge(hi_ready, k + 2)
                nc.vector.tensor_tensor(lo[:, k % 2], tab[:, k % LOADS], hi[:, k % 2].bitcast(F32), ALU.subtract)\
                    .then_inc(lo_ready, 1)

            def relu2(t):
                dve.wait_ge(l2_ready, t + 1)
                if t >= 2:
                    dve.wait_ge(l3_ready, t - 1)
                for n in range(M2):
                    last = nc.vector.tensor_scalar(h2[:, t % 2, n, :], ps_mlp[:, 1, n * TILE:(n + 1) * TILE],
                                                   b2_sb[:, n:n + 1], 0.0, ALU.add, ALU.max)
                last.then_inc(h2_placed, 1)

            def y_copy(t):
                dve.wait_ge(l3_ready, t + 1)
                copy(y[:, t * TILE:(t + 1) * TILE], ps_mlp[0:1, 1, M2 * TILE:(M2 + 1) * TILE])\
                    .then_inc(y_ready, 1)

            dve.wait_ge(s_dense, 16)
            copy(fields_t[:, :, 0], dense_sb[:]).then_inc(dense_placed, 1)
            for step, n, m in SCHEDULE:
                if step == "turn" and n % 2 == 0:
                    copy_turned(dve, copy, n)
                if step == "turn" and n == WD_AFTER:
                    dve.wait_ge(s_w1, 64)
                    dve.wait_ge(s_w2, 48)
                    nc.vector.tensor_tensor(wd[:], wd[:], wd_b[:], ALU.add).then_inc(wd_ready, 1)
                if step == "gram" and n % 2 == 0:
                    spread_grams(dve, copy, n)
                if step == "gram" and n == UNITS - 1:
                    spread_grams(dve, copy, n, 0, 1)
                if step == "layer1" and n == TILES - 1 and m % 2 == 0:
                    dve.wait_ge(l1_ready, n + m + 1)
                    nc.vector.tensor_scalar(h1[:, n % 2, m, :], ps_gram[:, m // 2, m % 2, 0:TILE],
                                            b1_sb[:, m:m + 1], 0.0, ALU.add, ALU.max).then_inc(h1_last[0], 1)
                if step == "layer2":
                    relu2(n)
                if step == "layer3":
                    y_copy(n)
            t = TILES - 1
            dve.wait_ge(l2_ready, t + 1)
            nc.vector.tensor_scalar(h2[:, t % 2, 0, :], ps_turn[:, 0, 0:TILE // UNIT, :].rearrange("p f b -> p (f b)"),
                                    b2_sb[:, 0:1], 0.0, ALU.add, ALU.max).then_inc(h2_last[0], 1)
            dve.wait_ge(l3_ready, t + 1)
            copy(y[:, t * TILE:], ps_mlp[0:1, 0, 0:TILE]).then_inc(y_ready, 1)

        @block.tensor
        def _(pe):
            def copied(n):
                pe.wait_ge(turn_copied[n % 2], n // 2 + 1)

            def turn(n):
                if n >= 2:
                    copied(n - 2)
                gathers = range(n * PER_BANK, min((n + 1) * PER_BANK, GATHERS))
                if n < BANKS - 1:
                    pe.wait_ge(s_gather[n], 16 * PER_BANK)
                for m in gathers:
                    if m >= LAST_BANK:
                        pe.wait_ge(s_last_gather[m - LAST_BANK], 16)
                    i = BLOCKS * (m % PER_BANK)
                    last = nc.tensor.transpose(ps_turn[:, n % 2, i:i + BLOCKS, :], rows[:, m, :], ident[:])
                last.then_inc(turned, 1)

            def gram(u):
                if u == 0:
                    pe.wait_ge(lookup_copied, K)
                    pe.wait_ge(dense_placed, 1)
                if u >= 2:
                    pe.wait_ge(spread[u % 2], u // 2)
                copied(bank_of(u))
                if bank_of(u):
                    copied(bank_of(u) - 1)
                for s in range(UNIT):
                    at = (s % GB) * NJ
                    last = nc.tensor.matmul(ps_gram[0:N, u % 2, s // GB, at:at + NJ], fields_t[:, u * UNIT + s, :],
                                            fields_t[:, u * UNIT + s, 1:N], start=True, stop=True)
                    if u == UNITS - 1 and s == GB - 1:
                        last.then_inc(gram_ready, 1)
                last.then_inc(gram_ready, 1)

            def layer1_dense(t, m, o):
                nc.tensor.matmul(o, wd[:, m:H1:M1], dense_sb[:, t * TILE:(t + 1) * TILE], start=True, stop=False)

            def layer1_pairs(t, m, o):
                for c in range(CHUNKS):
                    last = nc.tensor.matmul(o, w_folded_sb[:, c, m:H1:M1], folded[:, c, t * TILE:(t + 1) * TILE],
                                            start=False, stop=(c == CHUNKS - 1))
                return last

            def features(t):
                for e in range(2):
                    pe.wait_ge(spread[e], spread_count(t, e))
                if t < TILES - 1:
                    pe.wait_ge(s_fold[t], 16 * len(PARTS))
                else:
                    pe.wait_ge(s_fold[t], 16 * (len(PARTS) - POOL_PARTS))
                    pe.wait_ge(s_fold_pool, 16 * POOL_PARTS)

            def layer2(t):
                if t == 0:
                    pe.wait_ge(s_w2, 48)
                else:
                    pe.wait_ge(y_ready, t)
                for n in range(M2):
                    for m in range(M1):
                        if n == 0:
                            pe.wait_ge(h1_placed, M1 * t + m + 1)
                        last = nc.tensor.matmul(ps_mlp[:, 1, n * TILE:(n + 1) * TILE], w2_sb[:, m, n:H2:M2],
                                                h1[:, t % 2, m, :], start=(m == 0), stop=(m == M1 - 1))
                last.then_inc(l2_ready, 1)

            def layer3(t):
                pe.wait_ge(h2_placed, t + 1)
                for n in range(M2):
                    last = nc.tensor.matmul(ps_mlp[0:1, 1, M2 * TILE:(M2 + 1) * TILE], w3_sb[:, n:n + 1],
                                            h2[:, t % 2, n, :], start=(n == 0), stop=(n == M2 - 1))
                last.then_inc(l3_ready, 1)

            def lookup(k):
                if k >= 2:
                    pe.wait_ge(lookup_copied, k - 1)
                pe.wait_ge(hi_ready, k + 2 if k else 1)
                for c in range(VC):
                    if k == 0 and c == VC // 2:
                        pe.wait_ge(hi_ready, 2)
                    if c < VC - VC_ACT:
                        pe.wait_ge(hot_v, (VC - VC_ACT) * k + c + 1)
                    elif c == VC - VC_ACT:
                        pe.wait_ge(hot_a, k + 1)
                    nc.tensor.matmul(ps_mlp[:, k % 2, :], hi[:, k % 2, c, :], hot[:, k % 2, c, :],
                                     start=(c == 0), stop=False)
                pe.wait_ge(lo_ready, k + 1)
                for c in range(VC):
                    last = nc.tensor.matmul(ps_mlp[:, k % 2, :], lo[:, k % 2, c, :], hot[:, k % 2, c, :],
                                            start=False, stop=(c == VC - 1))
                last.then_inc(looked_up, 1)

            for k in range(K):
                lookup(k)
                if k in EARLY_TURNS:
                    if k == EARLY_TURNS[0]:
                        pe.wait_ge(s_ident, 16)
                    turn(EARLY_TURNS.index(k))
            for step, n, m in SCHEDULE:
                if step == "turn" and n >= len(EARLY_TURNS):
                    turn(n)
                if step == "gram":
                    gram(n)
                if step == "layer1" and n < TILES - 1:
                    if m == 0:
                        if n == 0:
                            pe.wait_ge(s_w1, 64)
                            pe.wait_ge(wd_ready, 1)
                        else:
                            pe.wait_ge(h1_placed, M1 * n)
                        features(n)
                    o = ps_mlp[:, 0, m * TILE:(m + 1) * TILE]
                    layer1_dense(n, m, o)
                    last = layer1_pairs(n, m, o)
                    if m == M1 - 1:
                        last.then_inc(l1_ready, 1)
                if step == "dense":
                    for e in range(2):
                        pe.wait_ge(spread[e], spread_count(n, e))
                    for i in range(M1):
                        layer1_dense(n, i, ps_gram[:, i // 2, i % 2, 0:TILE])
                if step == "layer1" and n == TILES - 1:
                    if m == 0:
                        features(n)
                    layer1_pairs(n, m, ps_gram[:, m // 2, m % 2, 0:TILE]).then_inc(l1_ready, 1)
                if step == "layer2":
                    layer2(n)
                if step == "layer3":
                    layer3(n)

            t = TILES - 1
            for n in range(2):
                copied(BANKS - 2 + n)
            for m in range(M1):
                pe.wait_ge(h1_last[m % 2], m // 2 + 1)
                for n in range(M2):
                    last = nc.tensor.matmul(ps_turn[:, n, 0:TILE // UNIT, :], w2_sb[:, m, n:H2:M2],
                                            h1[:, t % 2, m, :], start=(m == 0), stop=(m == M1 - 1))
                    if m == M1 - 1:
                        last.then_inc(l2_ready, 1)
            pe.wait_ge(h1_placed, M1 * t)
            for n in range(M2):
                pe.wait_ge(h2_last[n], 1)
                last = nc.tensor.matmul(ps_mlp[0:1, 0, 0:TILE], w3_sb[:, n:n + 1], h2[:, t % 2, n, :],
                                        start=(n == 0), stop=(n == M2 - 1))
            last.then_inc(l3_ready, 1)


def kernel(**inputs):
    import numpy as np
    import concourse.bacc as bacc
    from concourse.bass_utils import run_bass_kernel_spmd

    tables = [np.asarray(inputs[f"tbl_{f}"]) for f in range(N_FIELDS)]
    w1 = np.asarray(inputs["W_top1"])
    w_folded = np.zeros((128, CHUNKS, H1), w1.dtype)
    first = np.cumsum([D] + [N - 1 - i for i in range(N)])

    def weights(q, row, n, c, j, i):
        for r in range(min(n, j - i)):
            a, b = sorted((SLOTS[i + r], SLOTS[j]))
            w_folded[32 * q + row + r, c] = w1[first[a] + b - a - 1]

    for j in range(1, SHORT + 1):
        weights((j - 1) // CHUNKS, 0, j, (j - 1) % CHUNKS, j, 0)
    for q, row, n, c, cs, j, i in PARTS:
        for e in range(cs):
            weights(q, row, n, c + e, j + e, i)
    ids = np.asarray(inputs["ids"])
    begins = np.cumsum([0] + [VOCAB[f] for f in GATHERED[:-1]]).astype(np.int32)

    def gather_order(a):
        return a.reshape(UNITS, UNIT, G).transpose(0, 2, 1).reshape(GATHERS, 128).T

    row = np.arange(128 * VC, dtype=np.int32).reshape(128, VC)
    arranged = {
        "dense_t": np.asarray(inputs["r_dense_features"]).T,
        "idx": np.concatenate([gather_order(ids[:, GATHERED]),
                               gather_order(np.broadcast_to(begins, (BATCH, G))), row], axis=1),
        "lookup_ids": ids[:, LOOKED_UP].T,
        "store": np.concatenate([tables[f] for f in GATHERED]),
        "w_dense_a": w1[:D],
        "w_dense_b": w1[-D:],
        "w_folded": w_folded,
        "b1": np.asarray(inputs["b_top1"]).reshape(128, M1),
        "w2": np.asarray(inputs["W_top2"]).reshape(128, M1, H2),
        "b2": np.asarray(inputs["b_top2"]).reshape(128, M2),
        "w3": np.asarray(inputs["W_top3"]).reshape(128, M2),
        "identity": np.eye(128, dtype=np.float32),
    }
    nc = bacc.Bacc("TRN2", target_bir_lowering=False, num_devices=1)
    arrays = {}

    def dram(name, a):
        arrays[name] = np.ascontiguousarray(a)
        return nc.dram_tensor(name, arrays[name].shape, mybir.dt.from_np(arrays[name].dtype),
                              kind="ExternalInput").ap()

    args = {name: dram(name, a) for name, a in arranged.items()}
    lookups = [dram(f"tbl_{f}", tables[f]) for f in LOOKED_UP]
    out = nc.dram_tensor("out", (1, BATCH), F32, kind="ExternalOutput").ap()
    tower(nc, tables=lookups, out=out, **args)
    result = run_bass_kernel_spmd(nc, [arrays], core_ids=[0])
    return result.results[0]["out"].reshape(BATCH, 1)
```
